# Optimizing a Trainium2 kernel written in Bass

```python
import numpy as np
import jax
import jax.numpy as jnp

def _softmax(x, axis=-1):
    return jax.nn.softmax(x, axis=axis)
def _gelu(x):
    return jax.nn.gelu(x, approximate=True)
def _silu(x):
    return jax.nn.silu(x)
def _sigmoid(x):
    return jax.nn.sigmoid(x)
def _layernorm(x, axis=-1, eps=1e-5):
    m = jnp.mean(x, axis=axis, keepdims=True)
    v = jnp.var(x, axis=axis, keepdims=True)
    return (x - m) / jnp.sqrt(v + eps)
def _scatter_add(tgt, idx, src, axis=0):
    return tgt.at[idx].add(src)
def _segment_sum(src, seg, n):
    return jax.ops.segment_sum(src, seg, n)

kernel_name = 'mk_conv_preact_d1_conv_nchw256_3c1864'

def setup_inputs(seed: int = 0):
    np.random.seed(seed)
    _w = jnp.asarray
    def _rec_inputs():
        import jax
        import jax.numpy as jnp
        _gk = jax.random.key(seed)
        x = 1.508e-05 + 1 * jax.random.normal(jax.random.fold_in(_gk, 1), (16, 256, 128, 128), jnp.float32)
        return x
    x = _rec_inputs()
    def _L0_conv_setup():
        import jax, jax.numpy as jnp
        import numpy as np
        HEIGHT = 128
        WIDTH = 128

        def dct_filter(n: int) -> jnp.ndarray:
            v = jnp.arange(n, dtype=jnp.float32)[:, None]
            j = jnp.arange(n, dtype=jnp.float32)[None, :]
            f = jnp.cos(jnp.pi * (0.5 + j) * v / n) / jnp.sqrt(jnp.float32(n))
            scale = jnp.where(v != 0, jnp.sqrt(jnp.float32(2.0)), jnp.float32(1.0))
            return f * scale
        key = jax.random.key(seed)
        x = jax.random.normal(key, (16, 256, HEIGHT, WIDTH), dtype=jnp.float32)
        return {'x': x}
    _L0_conv_all = _L0_conv_setup()
    _L0_conv_in = {k: v for k, v in _L0_conv_all.items() if k in ()}
    del _L0_conv_all

    return {
        "x": x,
    }

def reference(x):
    import jax
    import jax.numpy as jnp
    def _L0_conv_ref(x):
        import jax, jax.numpy as jnp
        import numpy as np
        HEIGHT = 128
        WIDTH = 128

        def dct_filter(n: int) -> jnp.ndarray:
            v = jnp.arange(n, dtype=jnp.float32)[:, None]
            j = jnp.arange(n, dtype=jnp.float32)[None, :]
            f = jnp.cos(jnp.pi * (0.5 + j) * v / n) / jnp.sqrt(jnp.float32(n))
            scale = jnp.where(v != 0, jnp.sqrt(jnp.float32(2.0)), jnp.float32(1.0))
            return f * scale
        B, C, H, W = x.shape
        Wx = dct_filter(W)
        Wy = dct_filter(H)
        y = jnp.einsum('bchw,vw->bchv', x, Wx)
        out = jnp.einsum('bchv,kh->bckv', y, Wy)
        return out

    def _gn(v, G=32, eps=1e-5):
        B_, C_, H_, W_ = v.shape
        g = v.reshape(B_, G, C_ // G, H_, W_)
        m = jnp.mean(g, axis=(2, 3, 4), keepdims=True)
        s = jnp.var(g, axis=(2, 3, 4), keepdims=True)
        return ((g - m) / jnp.sqrt(s + eps)).reshape(v.shape)

    def _ln_c(v, eps=1e-6):
        m = jnp.mean(v, axis=1, keepdims=True)
        s = jnp.var(v, axis=1, keepdims=True)
        return (v - m) / jnp.sqrt(s + eps)

    def _ln_t(v, eps=1e-5):
        m = jnp.mean(v, axis=-1, keepdims=True)
        s = jnp.var(v, axis=-1, keepdims=True)
        return (v - m) / jnp.sqrt(s + eps)

    def _to_tokens(v):
        B_, C_, H_, W_ = v.shape
        return v.reshape(B_, C_, H_ * W_).transpose(0, 2, 1)
    def _from_tokens(t, like):
        B_, C_, H_, W_ = like.shape
        return t.transpose(0, 2, 1).reshape(B_, C_, H_, W_)

    x = x + _L0_conv_ref(_gn(x))
    return x


_drawn_inputs = setup_inputs


def setup_inputs(seed=0):
    import zlib

    import numpy as np

    out = dict(_drawn_inputs(seed))
    spreads = {}
    factors = {}
    for name, (base, spread) in spreads.items():
        noise = np.random.default_rng([zlib.crc32(name.encode()), seed]).standard_normal(out[name].shape)
        drawn = base * np.exp(spread * noise) if base else spread * noise
        out[name] = jnp.asarray(drawn.astype(out[name].dtype))
    for name, factor in factors.items():
        out[name] = (out[name] * factor).astype(out[name].dtype)
    return out
```

```python
from contextlib import ExitStack

import concourse.bass as bass
import numpy as np
from concourse import mybir

F32 = mybir.dt.float32
F16 = mybir.dt.float16
ALU = mybir.AluOpType
ACT = mybir.ActivationFunctionType
AXIS_X = mybir.AxisListType.X
SUM = bass.bass_isa.ReduceOp.add

P = 128
IMAGES = 8
COLS = IMAGES * P
BANK = 512
EPS = 1e-5
GAIN = 64.0

PAIR = 2
BATCH = 8
RING = 32
LOAD_AHEAD = 26
STATS_AHEAD = 20
SHORT = 4
NORM_AHEAD = 3
SPLIT_AHEAD = 2
CHAIN_AHEAD = 11
STAGE2_LAG = 2
CHAIN = 12


def dct_rows(n):
    v = np.arange(n, dtype=np.float32)[:, None]
    j = np.arange(n, dtype=np.float32)[None, :]
    f = np.cos(np.float32(np.pi) * (np.float32(0.5) + j) * v / np.float32(n)) / np.sqrt(np.float32(n))
    return (f * np.where(v != 0, np.sqrt(np.float32(2.0)), np.float32(1.0))).astype(np.float32)


def build(nc, x, dct_t, out):
    groups = x.shape[0] * x.shape[1] // IMAGES
    iterations = groups // RING
    assert groups % RING == 0 and iterations >= 2
    groups_in = x.rearrange("b (g c) h w -> (b g) h c w", c=IMAGES)
    pairs_out = out.rearrange("b (q c) h w -> (b q) h c w", c=PAIR * IMAGES)

    with ExitStack() as ctx:

        def sbuf(name, shape, dt):
            return ctx.enter_context(nc.sbuf_tensor(name, shape, dt))

        def psum(name, shape):
            return ctx.enter_context(nc.psum_tensor(name, shape, F32))

        def sem(name):
            return ctx.enter_context(nc.semaphore(name))

        x_ring = sbuf("x_ring", [P, RING, COLS], F32)
        xn = sbuf("xn", [P, SHORT, COLS], F32)
        xh = sbuf("xh", [P, SHORT, COLS], F16)
        xl = sbuf("xl", [P, SHORT, COLS], F16)
        th = sbuf("th", [P, SHORT, COLS], F16)
        tl = sbuf("tl", [P, SHORT, COLS], F16)
        dct = sbuf("dct", [P, P], F32)
        dh = sbuf("dh", [P, P], F16)
        dl = sbuf("dl", [P, P], F16)

        parts = COLS // 256
        part_stats = sbuf("part_stats", [P, 2, BATCH, parts, 3], F32)
        sum_of_means = sbuf("sum_of_means", [P, BATCH], F32)
        total_of_means = sbuf("total_of_means", [P, BATCH], F32)
        mean = sbuf("mean", [P, BATCH], F32)
        deviation = sbuf("deviation", [P, BATCH, parts], F32)
        square = sbuf("square", [P, BATCH, parts], F32)
        spread = sbuf("spread", [P, BATCH, parts], F32)
        sum_of_spreads = sbuf("sum_of_spreads", [P, BATCH], F32)
        total_of_spreads = sbuf("total_of_spreads", [P, BATCH], F32)
        var = sbuf("var", [P, BATCH], F32)
        root = sbuf("root", [P, BATCH], F32)
        guess = sbuf("guess", [P, BATCH], F32)
        guess2 = sbuf("guess2", [P, BATCH], F32)
        slack = sbuf("slack", [P, BATCH], F32)
        rstd = sbuf("rstd", [P, 2, BATCH], F32)
        shift = sbuf("shift", [P, 2, BATCH], F32)

        t_ps = [psum(f"t_ps{i}", [P, COLS]) for i in range(2)]
        y_ps = [psum(f"y_ps{i}", [P, COLS]) for i in range(2)]

        loaded = [sem(f"loaded{i}") for i in range(RING)]
        stored = [sem(f"stored{i}") for i in range(RING // PAIR)]
        dct_loaded = sem("dct_loaded")
        dct_split = sem("dct_split")
        bn_done = sem("bn_done")
        chain_done = sem("chain_done")
        reduced = sem("reduced")
        reducing = sem("reducing")
        root_done = sem("root_done")
        xn_done = sem("xn_done")
        xh_done = sem("xh_done")
        xl_done = sem("xl_done")
        t_done = sem("t_done")
        th_done = sem("th_done")
        tl_done = sem("tl_done")
        y_done = sem("y_done")
        out_done = sem("out_done")

        block = ctx.enter_context(nc.Block())

        def over_steps(engine, step, first=-STATS_AHEAD):
            for j in range(first, RING):
                step(0, j)
            if iterations > 2:
                with engine.Fori(1, iterations - 1) as it:
                    for j in range(RING):
                        step(it, j)
            for j in range(RING + STAGE2_LAG):
                step(iterations - 1, j)

        def inside(it, j):
            return not isinstance(it, int) or 0 <= it * RING + j < groups

        def slot(j):
            return j % RING

        @block.sync
        def _(sp):
            def load(it, j):
                s = slot(j)
                if s % PAIR == 0 and inside(it, j - RING):
                    sp.wait_ge(stored[s // PAIR], (it + j // RING) * 16)
                sp.dma_start(x_ring[:, s, :].rearrange("p (i w) -> p i w", w=P),
                             groups_in[it * RING + j]).then_inc(loaded[s], 16)

            def store(it, j):
                s = slot(j) // PAIR
                sp.wait_ge(out_done, it * RING + j + 1)
                sp.dma_start(
                    pairs_out[it * (RING // PAIR) + j // PAIR],
                    x_ring[:, s * PAIR:(s + 1) * PAIR, :].rearrange("p g (i w) -> p (g i) w", w=P),
                ).then_inc(stored[s], 16)

            def step(it, j):
                if j % PAIR == PAIR - 1:
                    if inside(it, j):
                        store(it, j)
                    for ahead in range(j + LOAD_AHEAD + 1 - PAIR, j + LOAD_AHEAD + 1):
                        if inside(it, ahead):
                            load(it, ahead)

            sp.dma_start(dct[:, :], dct_t).then_inc(dct_loaded, 16)
            over_steps(sp, step, -LOAD_AHEAD)
            for s in range(RING // PAIR):
                sp.wait_ge(stored[s], iterations * 16)

        @block.vector
        def _(dve):
            dve.wait_ge(dct_loaded, 16)
            nc.vector.tensor_scalar(dh[:, :], dct[:, :], GAIN, None, ALU.mult).then_inc(dct_split, 1)
            dve.wait_ge(dct_split, 1)
            nc.vector.scalar_tensor_tensor(out=dl[:, :], in0=dct[:, :], scalar=GAIN, in1=dh[:, :],
                                           op0=ALU.mult, op1=ALU.subtract).then_inc(dct_split, 1)

            def group_stats(it, j):
                s = slot(j)
                dve.wait_ge(loaded[s], (it + j // RING + 1) * 16)
                if s % BATCH == 0 and inside(it, j - 2 * BATCH):
                    dve.wait_ge(chain_done, (it * (RING // BATCH) + j // BATCH - 2) * CHAIN + 5)
                into = part_stats[:, (s // BATCH) % 2, s % BATCH, :, :].rearrange("p (c e) k -> p c (e k)", c=2)
                for c in range(2):
                    last = nc.vector.bn_stats(into[:, c, :], x_ring[:, s, c * BANK:(c + 1) * BANK])
                last.then_inc(bn_done, 1)

            def stats_chain(it, j, step):
                b = (j // BATCH) % 2
                batch = it * (RING // BATCH) + j // BATCH
                means, spreads = part_stats[:, b, :, :, 1], part_stats[:, b, :, :, 2]
                if step == 0:
                    dve.wait_ge(bn_done, it * RING + j + BATCH)
                else:
                    dve.wait_ge(chain_done, batch * CHAIN + step)
                if step == 0:
                    last = nc.vector.tensor_reduce(sum_of_means[:, :], means, AXIS_X, ALU.add)
                elif step == 1:
                    dve.wait_ge(reduced, batch * 2 + 1)
                    last = nc.vector.tensor_scalar(mean[:, :], total_of_means[:, :], 1.0 / (P * parts), None,
                                                   ALU.mult)
                elif step == 2:
                    last = nc.vector.tensor_tensor(
                        deviation[:, :, :], means, mean[:, :].unsqueeze(2).broadcast_to([P, BATCH, parts]),
                        ALU.subtract)
                elif step == 3:
                    last = nc.vector.scalar_tensor_tensor(
                        out=square[:, :, :], in0=deviation[:, :, :], scalar=float(COLS // parts),
                        in1=deviation[:, :, :], op0=ALU.mult, op1=ALU.mult)
                elif step == 4:
                    last = nc.vector.tensor_tensor(spread[:, :, :], square[:, :, :], spreads, ALU.add)
                elif step == 5:
                    last = nc.vector.tensor_reduce(sum_of_spreads[:, :], spread[:, :, :], AXIS_X, ALU.add)
                elif step == 6:
                    dve.wait_ge(reduced, batch * 2 + 2)
                    last = nc.vector.tensor_scalar(var[:, :], total_of_spreads[:, :],
                                                   1.0 / (P * COLS * GAIN**2), EPS / GAIN**2, ALU.mult, ALU.add)
                elif step == 7:
                    dve.wait_ge(root_done, batch + 1)
                    last = nc.vector.reciprocal(guess[:, :], root[:, :])
                elif step == 8:
                    last = nc.vector.tensor_tensor(guess2[:, :], guess[:, :], guess[:, :], ALU.mult)
                elif step == 9:
                    last = nc.vector.scalar_tensor_tensor(out=slack[:, :], in0=guess2[:, :], scalar=-0.5,
                                                          in1=var[:, :], op0=ALU.mult, op1=ALU.mult)
                elif step == 10:
                    if inside(it, j - 2 * BATCH):
                        dve.wait_ge(xn_done, it * RING + j - BATCH)
                    last = nc.vector.scalar_tensor_tensor(out=rstd[:, b, :], in0=slack[:, :], scalar=1.5,
                                                          in1=guess[:, :], op0=ALU.add, op1=ALU.mult)
                elif step == 11:
                    last = nc.vector.scalar_tensor_tensor(out=shift[:, b, :], in0=mean[:, :], scalar=-1.0,
                                                          in1=rstd[:, b, :], op0=ALU.mult, op1=ALU.mult)
                last.then_inc(chain_done, 1)

            def low_part(it, j):
                dve.wait_ge(th_done, it * RING + j + 1)
                if inside(it, j - SHORT):
                    dve.wait_ge(y_done, it * RING + j + 1 - SHORT)
                nc.vector.scalar_tensor_tensor(out=tl[:, j % SHORT, :], in0=t_ps[j % 2][:, :], scalar=1.0 / GAIN,
                                               in1=th[:, j % SHORT, :], op0=ALU.mult,
                                               op1=ALU.subtract).then_inc(tl_done, 1)

            def residual(it, j):
                s = slot(j)
                dve.wait_ge(y_done, it * RING + j + 1)
                nc.vector.scalar_tensor_tensor(out=x_ring[:, s, :], in0=y_ps[j % 2][:, :], scalar=1.0 / GAIN**2,
                                               in1=x_ring[:, s, :], op0=ALU.mult, op1=ALU.add).then_inc(out_done, 1)

            places = {(5, 0): 0, (7, 0): 1, (7, 1): 2, (7, 2): 3, (0, 0): 4, (0, 1): 5, (2, 0): 6, (3, 1): 7,
                      (3, 2): 8, (4, 0): 9, (4, 1): 10, (4, 2): 11}

            def chain_at(it, j, place):
                start = (j + CHAIN_AHEAD) // BATCH * BATCH
                if (j % BATCH, place) in places and inside(it, start):
                    stats_chain(it, start, places[j % BATCH, place])

            def step(it, j):
                chain_at(it, j, 0)
                if inside(it, j):
                    low_part(it, j)
                chain_at(it, j, 1)
                if inside(it, j + STATS_AHEAD):
                    group_stats(it, j + STATS_AHEAD)
                chain_at(it, j, 2)
                if inside(it, j - STAGE2_LAG):
                    residual(it, j - STAGE2_LAG)

            over_steps(dve, step)

        @block.scalar
        def _(act):
            def normalise(it, j):
                s, b = slot(j), (j // BATCH) % 2
                if s % BATCH == 0:
                    act.wait_ge(chain_done, (it * (RING // BATCH) + j // BATCH + 1) * CHAIN)
                if inside(it, j - SHORT):
                    act.wait_ge(xl_done, it * RING + j + 1 - SHORT)
                nc.scalar.activation(xn[:, j % SHORT, :], x_ring[:, s, :], ACT.Identity,
                                     bias=shift[:, b, s % BATCH:s % BATCH + 1],
                                     scale=rstd[:, b, s % BATCH:s % BATCH + 1]).then_inc(xn_done, 1)

            def high_of_x(it, j):
                act.wait_ge(xn_done, it * RING + j + 1)
                if inside(it, j - SHORT):
                    act.wait_ge(t_done, it * RING + j + 1 - SHORT)
                nc.scalar.activation(xh[:, j % SHORT, :], xn[:, j % SHORT, :], ACT.Identity).then_inc(xh_done, 1)

            def high_of_t(it, j):
                act.wait_ge(t_done, it * RING + j + 1)
                if inside(it, j - SHORT):
                    act.wait_ge(y_done, it * RING + j + 1 - SHORT)
                nc.scalar.activation(th[:, j % SHORT, :], t_ps[j % 2][:, :], ACT.Identity,
                                     scale=1.0 / GAIN).then_inc(th_done, 1)

            def step(it, j):
                if inside(it, j):
                    high_of_t(it, j)
                if inside(it, j + SPLIT_AHEAD):
                    high_of_x(it, j + SPLIT_AHEAD)
                if inside(it, j + NORM_AHEAD):
                    normalise(it, j + NORM_AHEAD)
                start = (j + CHAIN_AHEAD) // BATCH * BATCH
                if j % BATCH == 2 and inside(it, start):
                    act.wait_ge(chain_done, (it * (RING // BATCH) + start // BATCH) * CHAIN + 7)
                    nc.scalar.activation(root[:, :], var[:, :], ACT.Sqrt).then_inc(root_done, 1)

            over_steps(act, step)

        @block.gpsimd
        def _(pool):
            def low_of_x(it, j):
                pool.wait_ge(xh_done, it * RING + j + 1)
                if inside(it, j - SHORT):
                    pool.wait_ge(t_done, it * RING + j + 1 - SHORT)
                nc.gpsimd.tensor_tensor(xl[:, j % SHORT, :], xn[:, j % SHORT, :], xh[:, j % SHORT, :],
                                        ALU.subtract).then_inc(xl_done, 1)

            def over_partitions(it, j, step, total, part):
                pool.wait_ge(chain_done, (it * (RING // BATCH) + j // BATCH) * CHAIN + step + 1)
                pool.sem_inc(reducing)
                nc.gpsimd.partition_all_reduce(total[:, :], part[:, :], P, SUM).then_inc(reduced, 1)

            def step(it, j):
                start = (j + CHAIN_AHEAD) // BATCH * BATCH
                if j % BATCH == 6 and inside(it, start):
                    over_partitions(it, start, 0, total_of_means, sum_of_means)
                if j % BATCH == 1 and inside(it, start):
                    over_partitions(it, start, 5, total_of_spreads, sum_of_spreads)
                if inside(it, j + SPLIT_AHEAD):
                    low_of_x(it, j + SPLIT_AHEAD)

            over_steps(pool, step)

        @block.tensor
        def _(pe):
            def stage(into, high, low):
                for i in range(IMAGES):
                    cols = slice(i * P, (i + 1) * P)
                    nc.tensor.matmul(into[:, cols], high[:, cols], dh[:, :], start=True, stop=False)
                    nc.tensor.matmul(into[:, cols], high[:, cols], dl[:, :], start=False, stop=False)
                    last = nc.tensor.matmul(into[:, cols], low[:, cols], dh[:, :], start=False, stop=True)
                return last

            def stage1(it, j):
                pe.wait_ge(xl_done, it * RING + j + 1)
                if inside(it, j - 2):
                    pe.wait_ge(tl_done, it * RING + j - 1)
                stage(t_ps[j % 2], xh[:, j % SHORT, :], xl[:, j % SHORT, :]).then_inc(t_done, 1)

            def stage2(it, j):
                pe.wait_ge(tl_done, it * RING + j + 1)
                if inside(it, j - 2):
                    pe.wait_ge(out_done, it * RING + j - 1)
                stage(y_ps[j % 2], th[:, j % SHORT, :], tl[:, j % SHORT, :]).then_inc(y_done, 1)

            def step(it, j):
                if inside(it, j):
                    stage1(it, j)
                if inside(it, j - STAGE2_LAG):
                    stage2(it, j - STAGE2_LAG)

            pe.wait_ge(dct_split, 2)
            over_steps(pe, step)


def kernel(x):
    from concourse import bacc
    from concourse.bass_utils import run_bass_kernel_spmd

    x = np.ascontiguousarray(x)
    dct_t = np.ascontiguousarray(dct_rows(P).T)
    nc = bacc.Bacc("TRN2", target_bir_lowering=False, num_devices=1)
    x_dram = nc.dram_tensor("x_dram", x.shape, F32, kind="ExternalInput").ap()
    dct_dram = nc.dram_tensor("dct_dram", dct_t.shape, F32, kind="ExternalInput").ap()
    out_dram = nc.dram_tensor("out_dram", x.shape, F32, kind="ExternalOutput").ap()
    build(nc, x_dram, dct_dram, out_dram)
    done = run_bass_kernel_spmd(nc, [{"x_dram": x, "dct_dram": dct_t}], core_ids=[0])
    return done.results[0]["out_dram"]
```

```python
from contextlib import ExitStack

import concourse.bass as bass
import numpy as np
from concourse import mybir

F32 = mybir.dt.float32
F16 = mybir.dt.float16
ALU = mybir.AluOpType
ACT = mybir.ActivationFunctionType
AXIS_X = mybir.AxisListType.X
AXIS_XY = mybir.AxisListType.XY
SUM = bass.bass_isa.ReduceOp.add

P = 128
IMAGES = 8
COLS = IMAGES * P
BANK = 512
EPS = 1e-5
GAIN = 64.0

PAIR = 2
BATCH = 8
RING = 32
LOAD_AHEAD = 26
SHORT = 8
T_RING = 2
NORM_AHEAD = 3
POOL_NORM_AHEAD = 3
SPLIT_AHEAD = 2
STAGE2_LAG = 1
XN_BY_GPSIMD = (1, 3, 5, 7)
TL_BY_SCALAR = (0, 2, 4, 6)
CHAIN_PLACES = {(0, 0): [0], (2, 0): [1], (2, 1): [2], (2, 2): [3], (4, 2): [4], (6, 0): [5], (6, 1): [6], (6, 2): [7],
                (7, 0): [8], (7, 1): [9]}
REDUCE_PLACES = (1, 4)
ROOT_PLACE = 5
CHAIN_STEPS = 8
CHAIN_AHEAD = NORM_AHEAD + CHAIN_STEPS
STATS_AHEAD = CHAIN_AHEAD + BATCH
CHAIN = 10


def dct_rows(n):
    v = np.arange(n, dtype=np.float32)[:, None]
    j = np.arange(n, dtype=np.float32)[None, :]
    f = np.cos(np.float32(np.pi) * (np.float32(0.5) + j) * v / np.float32(n)) / np.sqrt(np.float32(n))
    return (f * np.where(v != 0, np.sqrt(np.float32(2.0)), np.float32(1.0))).astype(np.float32)


def build(nc, x, dct_t, out):
    groups = x.shape[0] * x.shape[1] // IMAGES
    iterations = groups // RING
    assert groups % RING == 0 and iterations >= 2
    groups_in = x.rearrange("b (g c) h w -> (b g) h c w", c=IMAGES)
    pairs_out = out.rearrange("b (q c) h w -> (b q) h c w", c=PAIR * IMAGES)

    with ExitStack() as ctx:

        def sbuf(name, shape, dt):
            return ctx.enter_context(nc.sbuf_tensor(name, shape, dt))

        def psum(name, shape):
            return ctx.enter_context(nc.psum_tensor(name, shape, F32))

        def sem(name):
            return ctx.enter_context(nc.semaphore(name))

        x_ring = sbuf("x_ring", [P, RING, COLS], F32)
        xn = sbuf("xn", [P, SHORT, COLS], F32)
        xh = sbuf("xh", [P, SHORT, COLS], F16)
        xl = sbuf("xl", [P, SHORT, COLS], F16)
        th = sbuf("th", [P, T_RING, COLS], F16)
        tl = sbuf("tl", [P, T_RING, COLS], F16)
        dct = sbuf("dct", [P, P], F32)
        dh = sbuf("dh", [P, P], F16)
        dl = sbuf("dl", [P, P], F16)
        minus_gain = sbuf("minus_gain", [P, P], F16)

        parts = COLS // 256
        part_stats = sbuf("part_stats", [P, 2, BATCH, parts, 3], F32)
        sum_of_means = sbuf("sum_of_means", [P, BATCH], F32)
        total_of_means = sbuf("total_of_means", [P, BATCH], F32)
        deviation = sbuf("deviation", [P, BATCH, parts], F32)
        sum_of_spreads = sbuf("sum_of_spreads", [P, BATCH], F32)
        total_of_spreads = sbuf("total_of_spreads", [P, BATCH], F32)
        var = sbuf("var", [P, BATCH], F32)
        root = sbuf("root", [P, BATCH], F32)
        guess = sbuf("guess", [P, BATCH], F32)
        guess2 = sbuf("guess2", [P, BATCH], F32)
        slack = sbuf("slack", [P, BATCH], F32)
        rstd = sbuf("rstd", [P, 2, BATCH], F32)
        shift = sbuf("shift", [P, 2, BATCH], F32)

        t_ps = [psum(f"t_ps{i}", [P, COLS]) for i in range(2)]
        y_ps = [psum(f"y_ps{i}", [P, COLS]) for i in range(2)]

        loaded = [sem(f"loaded{i}") for i in range(RING)]
        stored = [sem(f"stored{i}") for i in range(RING // PAIR)]
        dct_loaded = sem("dct_loaded")
        dct_split = sem("dct_split")
        diagonal_done = sem("diagonal_done")
        bn_done = sem("bn_done")
        chain_done = sem("chain_done")
        reduced = sem("reduced")
        waits_passed = sem("waits_passed")
        root_done = sem("root_done")
        xn_done = [sem("xn_by_scalar"), sem("xn_by_gpsimd")]
        xh_done = sem("xh_done")
        xl_done = sem("xl_done")
        t_done = sem("t_done")
        th_done = sem("th_done")
        t_less_th = sem("t_less_th")
        tl_done = [sem("tl_by_vector"), sem("tl_by_scalar")]
        y_done = sem("y_done")
        out_done = sem("out_done")

        block = ctx.enter_context(nc.Block())

        def over_steps(engine, step, first=-STATS_AHEAD):
            for j in range(first, RING):
                step(0, j)
            if iterations > 2:
                with engine.Fori(1, iterations - 1) as it:
                    for j in range(RING):
                        step(it, j)
            for j in range(RING + STAGE2_LAG):
                step(iterations - 1, j)

        def inside(it, j):
            return not isinstance(it, int) or 0 <= it * RING + j < groups

        def slot(j):
            return j % RING

        def chain_batch(j):
            return (j + CHAIN_AHEAD) // BATCH * BATCH, (j + CHAIN_AHEAD) % BATCH

        def side(shared, j):
            return int(j % BATCH in shared)

        def alike(shared, it, j):
            members = [m for m in range(BATCH) if side(shared, m) == side(shared, j)]
            return (it * (RING // BATCH) + j // BATCH) * len(members) + sum(m <= j % BATCH for m in members)

        @block.sync
        def _(sp):
            def load(it, j):
                s = slot(j)
                if s % PAIR == 0 and inside(it, j - RING):
                    sp.wait_ge(stored[s // PAIR], (it + j // RING) * 16)
                sp.dma_start(x_ring[:, s, :].rearrange("p (i w) -> p i w", w=P),
                             groups_in[it * RING + j]).then_inc(loaded[s], 16)

            def store(it, j):
                s = slot(j) // PAIR
                sp.wait_ge(out_done, it * RING + j + 1)
                sp.dma_start(
                    pairs_out[it * (RING // PAIR) + j // PAIR],
                    x_ring[:, s * PAIR:(s + 1) * PAIR, :].rearrange("p g (i w) -> p (g i) w", w=P),
                ).then_inc(stored[s], 16)

            def step(it, j):
                if j % PAIR == PAIR - 1:
                    if inside(it, j):
                        store(it, j)
                    for ahead in range(j + LOAD_AHEAD + 1 - PAIR, j + LOAD_AHEAD + 1):
                        if inside(it, ahead):
                            load(it, ahead)

            sp.dma_start(dct[:, :], dct_t).then_inc(dct_loaded, 16)
            over_steps(sp, step, -LOAD_AHEAD)
            for s in range(RING // PAIR):
                sp.wait_ge(stored[s], iterations * 16)

        @block.vector
        def _(dve):
            dve.wait_ge(dct_loaded, 16)
            nc.vector.tensor_scalar(dh[:, :], dct[:, :], GAIN, None, ALU.mult).then_inc(dct_split, 1)
            dve.wait_ge(dct_split, 1)
            nc.vector.scalar_tensor_tensor(out=dl[:, :], in0=dct[:, :], scalar=GAIN, in1=dh[:, :],
                                           op0=ALU.mult, op1=ALU.subtract).then_inc(dct_split, 1)

            def group_stats(it, j):
                s = slot(j)
                dve.wait_ge(loaded[s], (it + j // RING + 1) * 16)
                if s % BATCH == 0 and inside(it, j - 2 * BATCH):
                    dve.wait_ge(chain_done, (it * (RING // BATCH) + j // BATCH - 2) * CHAIN + 4)
                into = part_stats[:, (s // BATCH) % 2, s % BATCH, :, :].rearrange("p (c e) k -> p c (e k)", c=2)
                for c in range(2):
                    last = nc.vector.bn_stats(into[:, c, :], x_ring[:, s, c * BANK:(c + 1) * BANK])
                last.then_inc(bn_done, 1)

            def stats_chain(it, j, step):
                b = (j // BATCH) % 2
                batch = it * (RING // BATCH) + j // BATCH
                kept = part_stats[:, b, :, :, :]
                if step == 0:
                    dve.wait_ge(bn_done, it * RING + j + BATCH)
                else:
                    dve.wait_ge(chain_done, batch * CHAIN + step)
                if step == 0:
                    last = nc.vector.tensor_reduce(sum_of_means[:, :], kept[:, :, :, 1], AXIS_X, ALU.add)
                elif step == 1:
                    dve.wait_ge(reduced, batch * 2 + 1)
                    last = nc.vector.scalar_tensor_tensor(
                        out=deviation[:, :, :], scalar=-1.0 / (P * parts),
                        in0=total_of_means[:, :].unsqueeze(2).broadcast_to([P, BATCH, parts]), in1=kept[:, :, :, 1],
                        op0=ALU.mult, op1=ALU.add)
                elif step == 2:
                    last = nc.vector.scalar_tensor_tensor(
                        out=kept[:, :, :, 0], in0=deviation[:, :, :], scalar=float(COLS // parts),
                        in1=deviation[:, :, :], op0=ALU.mult, op1=ALU.mult)
                elif step == 3:
                    last = nc.vector.tensor_reduce(sum_of_spreads[:, :], kept[:, :, :, 0:3:2], AXIS_XY, ALU.add)
                elif step == 4:
                    dve.wait_ge(reduced, batch * 2 + 2)
                    last = nc.vector.tensor_scalar(var[:, :], total_of_spreads[:, :],
                                                   1.0 / (P * COLS * GAIN**2), EPS / GAIN**2, ALU.mult, ALU.add)
                elif step == 5:
                    dve.wait_ge(root_done, batch + 1)
                    last = nc.vector.reciprocal(guess[:, :], root[:, :])
                elif step == 6:
                    last = nc.vector.tensor_tensor(guess2[:, :], guess[:, :], guess[:, :], ALU.mult)
                elif step == 7:
                    last = nc.vector.scalar_tensor_tensor(out=slack[:, :], in0=guess2[:, :], scalar=-0.5,
                                                          in1=var[:, :], op0=ALU.mult, op1=ALU.mult)
                elif step == 8:
                    if inside(it, j - 2 * BATCH):
                        dve.wait_ge(xn_done[0], (it * (RING // BATCH) + j // BATCH - 1) * (BATCH - len(XN_BY_GPSIMD)))
                        dve.wait_ge(xn_done[1], (it * (RING // BATCH) + j // BATCH - 1) * len(XN_BY_GPSIMD))
                    last = nc.vector.scalar_tensor_tensor(out=rstd[:, b, :], in0=slack[:, :], scalar=1.5,
                                                          in1=guess[:, :], op0=ALU.add, op1=ALU.mult)
                elif step == 9:
                    last = nc.vector.scalar_tensor_tensor(out=shift[:, b, :], in0=total_of_means[:, :],
                                                          scalar=-1.0 / (P * parts), in1=rstd[:, b, :],
                                                          op0=ALU.mult, op1=ALU.mult)
                last.then_inc(chain_done, 1)

            def low_part(it, j):
                dve.wait_ge(th_done, it * RING + j + 1)
                if inside(it, j - T_RING):
                    dve.wait_ge(y_done, it * RING + j + 1 - T_RING)
                nc.vector.scalar_tensor_tensor(out=tl[:, j % T_RING, :], in0=t_ps[j % 2][:, :], scalar=1.0 / GAIN,
                                               in1=th[:, j % T_RING, :], op0=ALU.mult,
                                               op1=ALU.subtract).then_inc(tl_done[0], 1)

            def residual(it, j):
                s = slot(j)
                dve.wait_ge(y_done, it * RING + j + 1)
                nc.vector.scalar_tensor_tensor(out=x_ring[:, s, :], in0=y_ps[j % 2][:, :], scalar=1.0 / GAIN**2,
                                               in1=x_ring[:, s, :], op0=ALU.mult, op1=ALU.add).then_inc(out_done, 1)

            def chain_at(it, j, place):
                batch_start, slots = chain_batch(j)
                for step in CHAIN_PLACES.get((slots, place), ()):
                    if inside(it, batch_start):
                        stats_chain(it, batch_start, step)

            def step(it, j):
                chain_at(it, j, 0)
                if not side(TL_BY_SCALAR, j) and inside(it, j):
                    low_part(it, j)
                chain_at(it, j, 1)
                if inside(it, j + STATS_AHEAD):
                    group_stats(it, j + STATS_AHEAD)
                chain_at(it, j, 2)
                if inside(it, j - STAGE2_LAG):
                    residual(it, j - STAGE2_LAG)
                chain_at(it, j, 3)

            over_steps(dve, step)

        @block.scalar
        def _(act):
            def normalise(it, j):
                s, b = slot(j), (j // BATCH) % 2
                if s % BATCH == 0:
                    act.wait_ge(chain_done, (it * (RING // BATCH) + j // BATCH + 1) * CHAIN)
                if inside(it, j - SHORT):
                    act.wait_ge(xl_done, it * RING + j + 1 - SHORT)
                nc.scalar.activation(xn[:, j % SHORT, :], x_ring[:, s, :], ACT.Identity,
                                     bias=shift[:, b, s % BATCH:s % BATCH + 1],
                                     scale=rstd[:, b, s % BATCH:s % BATCH + 1]).then_inc(xn_done[0], 1)

            def high_of_x(it, j):
                act.wait_ge(xn_done[side(XN_BY_GPSIMD, j)], alike(XN_BY_GPSIMD, it, j))
                if inside(it, j - SHORT):
                    act.wait_ge(t_done, 2 * (it * RING + j + 1 - SHORT))
                nc.scalar.activation(xh[:, j % SHORT, :], xn[:, j % SHORT, :], ACT.Identity).then_inc(xh_done, 1)

            def high_of_t(it, j):
                if inside(it, j - T_RING):
                    act.wait_ge(y_done, it * RING + j + 1 - T_RING)
                for bank in range(2):
                    act.wait_ge(t_done, 2 * (it * RING + j) + bank + 1)
                    cols = slice(bank * BANK, (bank + 1) * BANK)
                    last = nc.scalar.activation(th[:, j % T_RING, cols], t_ps[j % 2][:, cols], ACT.Identity,
                                                scale=1.0 / GAIN)
                last.then_inc(th_done, 1)

            def low_of_t(it, j):
                act.wait_ge(t_less_th, alike(TL_BY_SCALAR, it, j))
                nc.scalar.activation(tl[:, j % T_RING, :], t_ps[j % 2][:, :], ACT.Identity,
                                     scale=1.0 / GAIN).then_inc(tl_done[1], 1)

            def step(it, j):
                if inside(it, j):
                    high_of_t(it, j)
                if inside(it, j + SPLIT_AHEAD):
                    high_of_x(it, j + SPLIT_AHEAD)
                if side(TL_BY_SCALAR, j) and inside(it, j):
                    low_of_t(it, j)
                if not side(XN_BY_GPSIMD, j + NORM_AHEAD) and inside(it, j + NORM_AHEAD):
                    normalise(it, j + NORM_AHEAD)
                start, slots = chain_batch(j)
                if slots == ROOT_PLACE and inside(it, start):
                    act.wait_ge(chain_done, (it * (RING // BATCH) + start // BATCH) * CHAIN + 5)
                    nc.scalar.activation(root[:, :], var[:, :], ACT.Sqrt).then_inc(root_done, 1)

            over_steps(act, step)

        @block.gpsimd
        def _(pool):
            nc.gpsimd.memset(minus_gain[:, :], 0.0).then_inc(diagonal_done, 1)
            pool.wait_ge(diagonal_done, 1)
            nc.gpsimd.affine_select(out=minus_gain[:, :], in_=minus_gain[:, :], compare_op=ALU.not_equal, fill=-GAIN,
                                    base=0, pattern=[[-1, P]], channel_multiplier=1).then_inc(diagonal_done, 1)

            def pass_waits():
                pool.sem_inc(waits_passed)

            def normalise(it, j):
                s, b = slot(j), (j // BATCH) % 2
                pool.wait_ge(chain_done, (it * (RING // BATCH) + j // BATCH + 1) * CHAIN)
                if inside(it, j - SHORT):
                    pool.wait_ge(xl_done, it * RING + j + 1 - SHORT)
                pass_waits()
                nc.gpsimd.tensor_scalar(xn[:, j % SHORT, :], x_ring[:, s, :], rstd[:, b, s % BATCH:s % BATCH + 1],
                                        shift[:, b, s % BATCH:s % BATCH + 1], ALU.mult,
                                        ALU.add).then_inc(xn_done[1], 1)

            def low_of_x(it, j):
                pool.wait_ge(xh_done, it * RING + j + 1)
                if inside(it, j - SHORT):
                    pool.wait_ge(t_done, 2 * (it * RING + j + 1 - SHORT))
                nc.gpsimd.tensor_tensor(xl[:, j % SHORT, :], xn[:, j % SHORT, :], xh[:, j % SHORT, :],
                                        ALU.subtract).then_inc(xl_done, 1)

            def over_partitions(it, j, step, total, part):
                pool.wait_ge(chain_done, (it * (RING // BATCH) + j // BATCH) * CHAIN + step + 1)
                pass_waits()
                nc.gpsimd.partition_all_reduce(total[:, :], part[:, :], P, SUM).then_inc(reduced, 1)

            def step(it, j):
                start, slots = chain_batch(j)
                if slots == REDUCE_PLACES[0] and inside(it, start):
                    over_partitions(it, start, 0, total_of_means, sum_of_means)
                if slots == REDUCE_PLACES[1] and inside(it, start):
                    over_partitions(it, start, 3, total_of_spreads, sum_of_spreads)
                if side(XN_BY_GPSIMD, j + POOL_NORM_AHEAD) and inside(it, j + POOL_NORM_AHEAD):
                    normalise(it, j + POOL_NORM_AHEAD)
                if inside(it, j + SPLIT_AHEAD):
                    low_of_x(it, j + SPLIT_AHEAD)

            over_steps(pool, step)

        @block.tensor
        def _(pe):
            def stage(into, high, low, banks_done=None):
                for i in range(IMAGES):
                    cols = slice(i * P, (i + 1) * P)
                    nc.tensor.matmul(into[:, cols], high[:, cols], dh[:, :], start=i % 4 == 0, stop=False,
                                     skip_group_check=True)
                    nc.tensor.matmul(into[:, cols], high[:, cols], dl[:, :], start=False, stop=False,
                                     skip_group_check=True)
                    last = nc.tensor.matmul(into[:, cols], low[:, cols], dh[:, :], start=False, stop=True,
                                            skip_group_check=True)
                    if banks_done is not None and (i + 1) % (BANK // P) == 0:
                        last.then_inc(banks_done, 1)
                return last

            def stage1(it, j):
                pe.wait_ge(xl_done, it * RING + j + 1)
                if inside(it, j - 2):
                    pe.wait_ge(tl_done[side(TL_BY_SCALAR, j - 2)], alike(TL_BY_SCALAR, it, j - 2))
                stage(t_ps[j % 2], xh[:, j % SHORT, :], xl[:, j % SHORT, :], t_done)

            def stage2(it, j):
                pe.wait_ge(tl_done[side(TL_BY_SCALAR, j)], alike(TL_BY_SCALAR, it, j))
                if inside(it, j - 2):
                    pe.wait_ge(out_done, it * RING + j - 1)
                stage(y_ps[j % 2], th[:, j % T_RING, :], tl[:, j % T_RING, :]).then_inc(y_done, 1)

            def take_th_off(it, j):
                pe.wait_ge(th_done, it * RING + j + 1)
                for c in range(0, COLS, BANK):
                    last = nc.tensor.matmul(t_ps[j % 2][:, c:c + BANK], minus_gain[:, :], th[:, j % T_RING, c:c + BANK],
                                            start=False, stop=True, skip_group_check=True)
                last.then_inc(t_less_th, 1)

            def step(it, j):
                if inside(it, j):
                    stage1(it, j)
                if inside(it, j - STAGE2_LAG):
                    stage2(it, j - STAGE2_LAG)
                if side(TL_BY_SCALAR, j) and inside(it, j):
                    take_th_off(it, j)

            pe.wait_ge(dct_split, 2)
            pe.wait_ge(diagonal_done, 2)
            over_steps(pe, step)


def kernel(x):
    from concourse import bacc
    from concourse.bass_utils import run_bass_kernel_spmd

    x = np.ascontiguousarray(x)
    dct_t = np.ascontiguousarray(dct_rows(P).T)
    nc = bacc.Bacc("TRN2", target_bir_lowering=False, num_devices=1)
    x_dram = nc.dram_tensor("x_dram", x.shape, F32, kind="ExternalInput").ap()
    dct_dram = nc.dram_tensor("dct_dram", dct_t.shape, F32, kind="ExternalInput").ap()
    out_dram = nc.dram_tensor("out_dram", x.shape, F32, kind="ExternalOutput").ap()
    build(nc, x_dram, dct_dram, out_dram)
    done = run_bass_kernel_spmd(nc, [{"x_dram": x, "dct_dram": dct_t}], core_ids=[0])
    return done.results[0]["out_dram"]
```
